# Optimizing a Trainium2 kernel written in Bass

```python
import numpy as np
import jax
import jax.numpy as jnp

def _softmax(x, axis=-1):
    return jax.nn.softmax(x, axis=axis)

def _gelu(x):
    return jax.nn.gelu(x, approximate=True)

def _silu(x):
    return jax.nn.silu(x)

def _sigmoid(x):
    return jax.nn.sigmoid(x)

def _layernorm(x, axis=-1, eps=1e-05):
    m = jnp.mean(x, axis=axis, keepdims=True)
    v = jnp.var(x, axis=axis, keepdims=True)
    return (x - m) / jnp.sqrt(v + eps)

def _scatter_add(tgt, idx, src, axis=0):
    return tgt.at[idx].add(src)

def _segment_sum(src, seg, n):
    return jax.ops.segment_sum(src, seg, n)
kernel_name = 'mk_dlrm_tower_d1_rec_r8_a5b8d8'

def setup_inputs(seed: int=0):
    np.random.seed(seed)
    _w = jnp.asarray

    def _rec_inputs():
        import jax
        import jax.numpy as jnp
        _tk = jax.random.key(seed)
        dense_ctx = jax.random.normal(jax.random.fold_in(_tk, 190), (512, 16), jnp.float32)
        ids = jnp.stack([jax.random.randint(jax.random.fold_in(_tk, 200 + f), (512,), 0, v, jnp.int32) for f, v in enumerate([1250, 1250, 1250, 1000, 12500, 12500, 1000, 1250, 125000, 1000, 1000, 1250, 1250, 1000, 12500, 12500, 1000, 12500, 1000, 125000, 12500, 1000, 1000, 12500, 1000, 12500, 12500, 1000, 1250, 12500, 1000, 12500])], axis=1)
        tbl_0 = 0.05 * jax.random.normal(jax.random.fold_in(_tk, 500 + 0), (1250, 64), jnp.float32)
        tbl_1 = 0.05 * jax.random.normal(jax.random.fold_in(_tk, 500 + 1), (1250, 64), jnp.float32)
        tbl_2 = 0.05 * jax.random.normal(jax.random.fold_in(_tk, 500 + 2), (1250, 64), jnp.float32)
        tbl_3 = 0.05 * jax.random.normal(jax.random.fold_in(_tk, 500 + 3), (1000, 64), jnp.float32)
        tbl_4 = 0.05 * jax.random.normal(jax.random.fold_in(_tk, 500 + 4), (12500, 64), jnp.float32)
        tbl_5 = 0.05 * jax.random.normal(jax.random.fold_in(_tk, 500 + 5), (12500, 64), jnp.float32)
        tbl_6 = 0.05 * jax.random.normal(jax.random.fold_in(_tk, 500 + 6), (1000, 64), jnp.float32)
        tbl_7 = 0.05 * jax.random.normal(jax.random.fold_in(_tk, 500 + 7), (1250, 64), jnp.float32)
        tbl_8 = 0.05 * jax.random.normal(jax.random.fold_in(_tk, 500 + 8), (125000, 64), jnp.float32)
        tbl_9 = 0.05 * jax.random.normal(jax.random.fold_in(_tk, 500 + 9), (1000, 64), jnp.float32)
        tbl_10 = 0.05 * jax.random.normal(jax.random.fold_in(_tk, 500 + 10), (1000, 64), jnp.float32)
        tbl_11 = 0.05 * jax.random.normal(jax.random.fold_in(_tk, 500 + 11), (1250, 64), jnp.float32)
        tbl_12 = 0.05 * jax.random.normal(jax.random.fold_in(_tk, 500 + 12), (1250, 64), jnp.float32)
        tbl_13 = 0.05 * jax.random.normal(jax.random.fold_in(_tk, 500 + 13), (1000, 64), jnp.float32)
        tbl_14 = 0.05 * jax.random.normal(jax.random.fold_in(_tk, 500 + 14), (12500, 64), jnp.float32)
        tbl_15 = 0.05 * jax.random.normal(jax.random.fold_in(_tk, 500 + 15), (12500, 64), jnp.float32)
        tbl_16 = 0.05 * jax.random.normal(jax.random.fold_in(_tk, 500 + 16), (1000, 64), jnp.float32)
        tbl_17 = 0.05 * jax.random.normal(jax.random.fold_in(_tk, 500 + 17), (12500, 64), jnp.float32)
        tbl_18 = 0.05 * jax.random.normal(jax.random.fold_in(_tk, 500 + 18), (1000, 64), jnp.float32)
        tbl_19 = 0.05 * jax.random.normal(jax.random.fold_in(_tk, 500 + 19), (125000, 64), jnp.float32)
        tbl_20 = 0.05 * jax.random.normal(jax.random.fold_in(_tk, 500 + 20), (12500, 64), jnp.float32)
        tbl_21 = 0.05 * jax.random.normal(jax.random.fold_in(_tk, 500 + 21), (1000, 64), jnp.float32)
        tbl_22 = 0.05 * jax.random.normal(jax.random.fold_in(_tk, 500 + 22), (1000, 64), jnp.float32)
        tbl_23 = 0.05 * jax.random.normal(jax.random.fold_in(_tk, 500 + 23), (12500, 64), jnp.float32)
        tbl_24 = 0.05 * jax.random.normal(jax.random.fold_in(_tk, 500 + 24), (1000, 64), jnp.float32)
        tbl_25 = 0.05 * jax.random.normal(jax.random.fold_in(_tk, 500 + 25), (12500, 64), jnp.float32)
        tbl_26 = 0.05 * jax.random.normal(jax.random.fold_in(_tk, 500 + 26), (12500, 64), jnp.float32)
        tbl_27 = 0.05 * jax.random.normal(jax.random.fold_in(_tk, 500 + 27), (1000, 64), jnp.float32)
        tbl_28 = 0.05 * jax.random.normal(jax.random.fold_in(_tk, 500 + 28), (1250, 64), jnp.float32)
        tbl_29 = 0.05 * jax.random.normal(jax.random.fold_in(_tk, 500 + 29), (12500, 64), jnp.float32)
        tbl_30 = 0.05 * jax.random.normal(jax.random.fold_in(_tk, 500 + 30), (1000, 64), jnp.float32)
        tbl_31 = 0.05 * jax.random.normal(jax.random.fold_in(_tk, 500 + 31), (12500, 64), jnp.float32)
        _rk = jax.random.fold_in(_tk, 7)
        W_top1 = 0.0441942 * jax.random.normal(jax.random.fold_in(_tk, 801), (512, 512), jnp.float32)
        W_top2 = 0.0441942 * jax.random.normal(jax.random.fold_in(_tk, 802), (512, 256), jnp.float32)
        W_top3 = 0.0625 * jax.random.normal(jax.random.fold_in(_tk, 803), (256, 1), jnp.float32)
        b_top1 = jnp.zeros((512,), jnp.float32)
        b_top2 = jnp.zeros((256,), jnp.float32)
        return (dense_ctx, ids, tbl_0, tbl_1, tbl_2, tbl_3, tbl_4, tbl_5, tbl_6, tbl_7, tbl_8, tbl_9, tbl_10, tbl_11, tbl_12, tbl_13, tbl_14, tbl_15, tbl_16, tbl_17, tbl_18, tbl_19, tbl_20, tbl_21, tbl_22, tbl_23, tbl_24, tbl_25, tbl_26, tbl_27, tbl_28, tbl_29, tbl_30, tbl_31, W_top1, b_top1, W_top2, b_top2, W_top3)
    dense_ctx, ids, tbl_0, tbl_1, tbl_2, tbl_3, tbl_4, tbl_5, tbl_6, tbl_7, tbl_8, tbl_9, tbl_10, tbl_11, tbl_12, tbl_13, tbl_14, tbl_15, tbl_16, tbl_17, tbl_18, tbl_19, tbl_20, tbl_21, tbl_22, tbl_23, tbl_24, tbl_25, tbl_26, tbl_27, tbl_28, tbl_29, tbl_30, tbl_31, W_top1, b_top1, W_top2, b_top2, W_top3 = _rec_inputs()

    def _L0_rec_setup():
        import jax, jax.numpy as jnp
        import numpy as np
        B = 256
        NUM_FIELDS = 32
        EMBED = 64
        P = NUM_FIELDS * (NUM_FIELDS - 1) // 2
        _ROW, _COL = np.triu_indices(NUM_FIELDS, k=1)
        ROW_IDX = jnp.asarray(_ROW, dtype=jnp.int32)
        COL_IDX = jnp.asarray(_COL, dtype=jnp.int32)
        key = jax.random.key(seed)
        k1, k2 = jax.random.split(key)
        emb_inputs = jax.random.normal(k1, (B, NUM_FIELDS, EMBED), dtype=jnp.float32)
        fan_in = P * EMBED
        fan_out = EMBED
        std = float(np.sqrt(2.0 / (fan_in + fan_out)))
        kernel = jax.random.normal(k2, (EMBED, P, EMBED), dtype=jnp.float32) * std
        return {'emb_inputs': emb_inputs, 'kernel': kernel}
    _L0_rec_all = _L0_rec_setup()
    _L0_rec_in = {k: v for k, v in _L0_rec_all.items() if k in ('kernel',)}
    del _L0_rec_all
    return {'dense_ctx': dense_ctx, 'ids': ids, 'tbl_0': tbl_0, 'tbl_1': tbl_1, 'tbl_2': tbl_2, 'tbl_3': tbl_3, 'tbl_4': tbl_4, 'tbl_5': tbl_5, 'tbl_6': tbl_6, 'tbl_7': tbl_7, 'tbl_8': tbl_8, 'tbl_9': tbl_9, 'tbl_10': tbl_10, 'tbl_11': tbl_11, 'tbl_12': tbl_12, 'tbl_13': tbl_13, 'tbl_14': tbl_14, 'tbl_15': tbl_15, 'tbl_16': tbl_16, 'tbl_17': tbl_17, 'tbl_18': tbl_18, 'tbl_19': tbl_19, 'tbl_20': tbl_20, 'tbl_21': tbl_21, 'tbl_22': tbl_22, 'tbl_23': tbl_23, 'tbl_24': tbl_24, 'tbl_25': tbl_25, 'tbl_26': tbl_26, 'tbl_27': tbl_27, 'tbl_28': tbl_28, 'tbl_29': tbl_29, 'tbl_30': tbl_30, 'tbl_31': tbl_31, 'W_top1': W_top1, 'b_top1': b_top1, 'W_top2': W_top2, 'b_top2': b_top2, 'W_top3': W_top3, 'L0_rec_kernel': _L0_rec_in['kernel']}

def reference(dense_ctx, ids, tbl_0, tbl_1, tbl_2, tbl_3, tbl_4, tbl_5, tbl_6, tbl_7, tbl_8, tbl_9, tbl_10, tbl_11, tbl_12, tbl_13, tbl_14, tbl_15, tbl_16, tbl_17, tbl_18, tbl_19, tbl_20, tbl_21, tbl_22, tbl_23, tbl_24, tbl_25, tbl_26, tbl_27, tbl_28, tbl_29, tbl_30, tbl_31, W_top1, b_top1, W_top2, b_top2, W_top3, L0_rec_kernel):
    import jax
    import jax.numpy as jnp

    def _L0_rec_ref(emb_inputs, kernel):
        import jax, jax.numpy as jnp
        import numpy as np
        B = 256
        NUM_FIELDS = 32
        EMBED = 64
        P = NUM_FIELDS * (NUM_FIELDS - 1) // 2
        _ROW, _COL = np.triu_indices(NUM_FIELDS, k=1)
        ROW_IDX = jnp.asarray(_ROW, dtype=jnp.int32)
        COL_IDX = jnp.asarray(_COL, dtype=jnp.int32)
        p = emb_inputs[:, ROW_IDX]
        q = emb_inputs[:, COL_IDX]
        return jnp.einsum('bne,hne,bnh->bn', p, kernel, q)
    e = jnp.stack([tbl_0[ids[:, 0]], tbl_1[ids[:, 1]], tbl_2[ids[:, 2]], tbl_3[ids[:, 3]], tbl_4[ids[:, 4]], tbl_5[ids[:, 5]], tbl_6[ids[:, 6]], tbl_7[ids[:, 7]], tbl_8[ids[:, 8]], tbl_9[ids[:, 9]], tbl_10[ids[:, 10]], tbl_11[ids[:, 11]], tbl_12[ids[:, 12]], tbl_13[ids[:, 13]], tbl_14[ids[:, 14]], tbl_15[ids[:, 15]], tbl_16[ids[:, 16]], tbl_17[ids[:, 17]], tbl_18[ids[:, 18]], tbl_19[ids[:, 19]], tbl_20[ids[:, 20]], tbl_21[ids[:, 21]], tbl_22[ids[:, 22]], tbl_23[ids[:, 23]], tbl_24[ids[:, 24]], tbl_25[ids[:, 25]], tbl_26[ids[:, 26]], tbl_27[ids[:, 27]], tbl_28[ids[:, 28]], tbl_29[ids[:, 29]], tbl_30[ids[:, 30]], tbl_31[ids[:, 31]]], axis=1)
    z = _L0_rec_ref(e, L0_rec_kernel)
    z = z.reshape(z.shape[0], -1)
    h = jnp.concatenate([z, dense_ctx], axis=1)
    h = jnp.maximum(h @ W_top1 + b_top1, 0.0)
    h = jnp.maximum(h @ W_top2 + b_top2, 0.0)
    y = h @ W_top3
    return y

_drawn_inputs = setup_inputs


def setup_inputs(seed=0):
    import zlib

    import numpy as np

    out = dict(_drawn_inputs(seed))
    spreads = {'b_top1': (0.0, 0.1), 'b_top2': (0.0, 0.1)}
    factors = {'tbl_0': 8.0,
     'tbl_1': 8.0,
     'tbl_2': 8.0,
     'tbl_3': 8.0,
     'tbl_4': 8.0,
     'tbl_5': 8.0,
     'tbl_6': 8.0,
     'tbl_7': 8.0,
     'tbl_8': 8.0,
     'tbl_9': 8.0,
     'tbl_10': 8.0,
     'tbl_11': 8.0,
     'tbl_12': 8.0,
     'tbl_13': 8.0,
     'tbl_14': 8.0,
     'tbl_15': 8.0,
     'tbl_16': 8.0,
     'tbl_17': 8.0,
     'tbl_18': 8.0,
     'tbl_19': 8.0,
     'tbl_20': 8.0,
     'tbl_21': 8.0,
     'tbl_22': 8.0,
     'tbl_23': 8.0,
     'tbl_24': 8.0,
     'tbl_25': 8.0,
     'tbl_26': 8.0,
     'tbl_27': 8.0,
     'tbl_28': 8.0,
     'tbl_29': 8.0,
     'tbl_30': 8.0,
     'tbl_31': 8.0,
     'L0_rec_kernel': 8.0}
    for name, (base, spread) in spreads.items():
        noise = np.random.default_rng([zlib.crc32(name.encode()), seed]).standard_normal(out[name].shape)
        drawn = base * np.exp(spread * noise) if base else spread * noise
        out[name] = jnp.asarray(drawn.astype(out[name].dtype))
    for name, factor in factors.items():
        out[name] = (out[name] * factor).astype(out[name].dtype)
    return out
```

```python
from contextlib import ExitStack

import numpy as np

import concourse.bass as bass
from concourse import mybir

F32 = mybir.dt.float32
F32R = mybir.dt.float32r
I32 = mybir.dt.int32
ALU = mybir.AluOpType
ACT = mybir.ActivationFunctionType

P = 128
FIELDS = 32
EMBED = 64
BATCH = 512
BT = BATCH // P
NK = FIELDS // 2
DENSE = 16
HID1, HID2 = 512, 256
M1, M2 = HID1 // P, HID2 // P

GROUPS = [(k, j) for k in range(NK) for j in range(k + 1)]
GROUP_C = [[2 * k, 2 * k + 1] if j < k else [2 * k + 1] for k, j in GROUPS]
TILES = [(g, i, c, GROUPS[g][1]) for g, cs in enumerate(GROUP_C) for i, c in enumerate(cs)]
FIRST_TILE = [next(t for t, x in enumerate(TILES) if x[0] == g) for g in range(len(GROUPS))]
NT = len(TILES)
GROUP_END = [sum(k + 1 for k in range(n + 1)) for n in range(NK)]

CHUNK = 16
BLOCKS = CHUNK // 2
NQ = NT // CHUNK
CC = BLOCKS * P

ZT = 64
NZ = NT // ZT
BATCH_T = 4

E_SLOTS, X_SLOTS, R_SLOTS, H_SLOTS, S_SLOTS, T_SLOTS, P_SLOTS = 4, 2, 3, 2, 5, 3, 8
SUM_LAG = 2
Z_LAG = 2
X_LEAD = 13


def z_row(t, i):
    return t // ZT, 32 * (t % BATCH_T) + 2 * ((t % ZT) // BATCH_T) + i


def tile_fields(t):
    _, _, c, j = TILES[t]
    return [(2 * j, c), (2 * j + 1, c)]


def turn(k):
    return 0 if k == 0 else max((k - 1) ** 2, k * k - X_LEAD)


def split_turn(q):
    return q - 10 if q < 2 else 2 * q - 3 if q < S_SLOTS else CHUNK * (q - S_SLOTS + 1) + 2


def dlrm_tower(nc, dense_z, ids, tables, k_tiles, w1, w2, w3, b1, b2, out):
    ctx = ExitStack()
    with ctx:
        def sb(name, shape, dt=F32):
            return ctx.enter_context(nc.sbuf_tensor(name, shape, dt))

        def ps(name, shape):
            return ctx.enter_context(nc.psum_tensor(name, shape, F32))

        def sem(name):
            return ctx.enter_context(nc.semaphore(name))

        ids_sb = sb("ids_sb", [P, BT, FIELDS], I32)
        emb = sb("emb", [P, E_SLOTS, BT, 2 * EMBED])
        ident = sb("ident", [P, P])
        ones_at = sb("ones_at", [P, 62])
        feat = sb("feat", [P, NK, BATCH])
        feat_hi = sb("feat_hi", [P, X_SLOTS, BATCH], F32R)
        feat_lo = sb("feat_lo", [P, X_SLOTS, BATCH], F32R)
        x_hi = sb("x_hi", [P, X_SLOTS, 2, BATCH], F32R)
        x_lo = sb("x_lo", [P, X_SLOTS, 2, BATCH], F32R)
        k_raw = sb("k_raw", [P, R_SLOTS, CC])
        k_hi = sb("k_hi", [P, H_SLOTS, CC], F32R)
        k_lo = sb("k_lo", [P, H_SLOTS, CC], F32R)
        k_st = sb("k_st", [P, S_SLOTS, 2, CC], F32R)
        prod = sb("prod", [P, P_SLOTS, 2, BATCH])
        dense_sb = sb("dense_sb", [P, NZ, BATCH])
        z_sb = sb("z_sb", [P, NZ, BATCH])
        w1_sb = sb("w1_sb", [P, NZ, HID1])
        w2_sb = sb("w2_sb", [P, M1, HID2])
        w3_sb = sb("w3_sb", [P, M2])
        b1_sb = sb("b1_sb", [P, M1])
        b2_sb = sb("b2_sb", [P, M2])
        h1_sb = sb("h1_sb", [P, M1, BATCH])
        h2_sb = sb("h2_sb", [P, M2, BATCH])
        y_sb = sb("y_sb", [1, BATCH])

        t_ps = ps("t_ps", [P, T_SLOTS, 2, BATCH])
        z_ps = ps("z_ps", [P, BATCH])
        f_ps = ps("f_ps", [P, BATCH])

        ids_loaded = sem("ids_loaded")
        consts_made = sem("consts_made")
        zeroed = sem("zeroed")
        gathered = [sem(f"gathered{i}") for i in range(E_SLOTS)]
        f_transposed = sem("f_transposed")
        f_copied = sem("f_copied")
        fl_made = sem("fl_made")
        xh_placed = sem("xh_placed")
        xl_placed = [sem(f"xl_placed{i}") for i in range(X_SLOTS)]
        k_loaded = [sem(f"k_loaded{i}") for i in range(R_SLOTS)]
        kh_made = sem("kh_made")
        kh_placed = sem("kh_placed")
        kl_made = sem("kl_made")
        kl_placed = [sem(f"kl_placed{i}") for i in range(S_SLOTS)]
        t_made = sem("t_made")
        p_made = sem("p_made")
        summed = sem("summed")
        z_made = sem("z_made")
        w_loaded = sem("w_loaded")
        h1_summed = sem("h1_summed")
        h1_made = sem("h1_made")
        h2_summed = sem("h2_summed")
        h2_made = sem("h2_made")
        y_summed = sem("y_summed")
        y_made = sem("y_made")
        y_stored = sem("y_stored")

        W_DMAS = 2 * NZ + 4

        def tiles_gone(eng, t):
            if t > 0:
                eng.wait_ge(t_made, TILES[t - 1][0] + 1)

        def x_slot_free(eng, k):
            if k >= X_SLOTS:
                eng.wait_ge(t_made, GROUP_END[k - X_SLOTS])

        block = ctx.enter_context(nc.Block())

        @block.sync
        def _(sp):
            sp.dma_start(ids_sb[:], ids.rearrange("(t p) f -> p t f", p=P)).then_inc(ids_loaded, 16)

            def load_k(q):
                if q >= R_SLOTS:
                    sp.wait_ge(kl_made, q - R_SLOTS + 1)
                    sp.wait_ge(kh_placed, 2 * (q - R_SLOTS + 1))
                sp.dma_start(k_raw[:, q % R_SLOTS, :], k_tiles[q]).then_inc(k_loaded[q % R_SLOTS], 16)

            def place_k_lo(q):
                sp.wait_ge(kl_made, q + 1)
                tiles_gone(sp, CHUNK * (q - S_SLOTS + 1))
                s, r = q % S_SLOTS, q % H_SLOTS
                for side, to, of in ((0, slice(64, 128), slice(0, 64)), (1, slice(0, 64), slice(64, 128))):
                    sp.dma_start(k_st[to, s, side, :].bitcast(F32),
                                 k_lo[of, r, :].bitcast(F32)).then_inc(kl_placed[s], 16)

            def place_x_lo(k):
                sp.wait_ge(fl_made, k + 1)
                x_slot_free(sp, k)
                s = k % X_SLOTS
                for i in range(2):
                    for to in (slice(0, 64), slice(64, 128)):
                        sp.dma_start(x_lo[to, s, i, :].bitcast(F32),
                                     feat_lo[64 * i:64 * i + 64, s, :].bitcast(F32)).then_inc(xl_placed[s], 16)

            weights = [(to[:, n, :], of[:, n, :]) for n in range(NZ) for to, of in ((dense_sb, dense_z), (w1_sb, w1))]
            weights += [(w2_sb[:], w2), (w3_sb[:], w3), (b1_sb[:], b1), (b2_sb[:], b2)]

            def load_weights():
                for to, of in weights[:2]:
                    sp.dma_start(to, of).then_inc(w_loaded, 16)
                del weights[:2]

            events = [(turn(k) + (2 if k > 7 else 0), 2, place_x_lo, k) for k in range(NK)]
            events += [(split_turn(q) + 3, 1, place_k_lo, q) for q in range(NQ)]
            events += [(-100 if q < R_SLOTS else split_turn(q - R_SLOTS) + 4, 0, load_k, q) for q in range(NQ)]
            for _, _, step, n in sorted(events, key=lambda x: (x[0], x[1], x[3])):
                step(n)
                if step is place_x_lo:
                    load_weights()
            sp.wait_ge(y_made, 1)
            sp.dma_start(out.rearrange("b o -> o b"), y_sb[:]).then_inc(y_stored, 16)
            sp.wait_ge(y_stored, 16)

        @block.gpsimd
        def _(pool):
            pool.wait_ge(zeroed, 1)
            nc.gpsimd.affine_select(out=ident[:], in_=ident[:], compare_op=ALU.not_equal, fill=1.0,
                                    base=0, pattern=[[-1, P]], channel_multiplier=1).then_inc(consts_made, 1)
            pool.wait_ge(ids_loaded, 16)
            for k in range(NK):
                if k >= E_SLOTS:
                    pool.wait_ge(f_transposed, k - E_SLOTS + 1)
                for i in range(2):
                    for t in range(BT):
                        f = 2 * k + i
                        pool.indirect_dma_start(
                            emb[:, k % E_SLOTS, t, EMBED * i:EMBED * (i + 1)], None, tables[f],
                            bass.IndirectOffsetOnAxis(ap=ids_sb[:, t, f:f + 1], axis=0),
                        ).then_inc(gathered[k % E_SLOTS], 16)

        @block.scalar
        def _(act):
            def split_x(k):
                s = k % X_SLOTS
                act.wait_ge(f_transposed, k + 1)
                if k >= X_SLOTS:
                    act.wait_ge(fl_made, k - X_SLOTS + 1)
                nc.scalar.activation(feat_hi[:, s, :], f_ps[:], ACT.Copy).then_inc(f_copied, 1)
                nc.scalar.activation(feat[:, k, :], f_ps[:], ACT.Copy).then_inc(f_copied, 1)
                x_slot_free(act, k)
                for i in range(2):
                    for to in (slice(0, 64), slice(64, 128)):
                        nc.scalar.activation(x_hi[to, s, i, :], f_ps[64 * i:64 * i + 64, :],
                                             ACT.Copy).then_inc(xh_placed, 1)

            def split_k(q):
                raw = k_raw[:, q % R_SLOTS, :]
                act.wait_ge(k_loaded[q % R_SLOTS], 16 * (q // R_SLOTS + 1))
                if q >= H_SLOTS:
                    act.wait_ge(kl_made, q - H_SLOTS + 1)
                nc.scalar.activation(k_hi[:, q % H_SLOTS, :], raw, ACT.Copy).then_inc(kh_made, 1)
                tiles_gone(act, CHUNK * (q - S_SLOTS + 1))
                for side, at in ((0, slice(0, 64)), (1, slice(64, 128))):
                    nc.scalar.activation(k_st[at, q % S_SLOTS, side, :], raw[at, :],
                                         ACT.Copy).then_inc(kh_placed, 1)

            events = [(turn(k), 1, split_x, k) for k in range(NK)]
            events += [(split_turn(q), 0, split_k, q) for q in range(NQ)]
            for _, _, step, n in sorted(events, key=lambda x: (x[0], x[1], x[3])):
                step(n)
            act.wait_ge(w_loaded, 16 * W_DMAS)
            for m in range(0, M1, 2):
                act.wait_ge(h1_summed, m + 1)
                nc.scalar.activation(h1_sb[:, m, :], t_ps[:, m // 2, m % 2, :], ACT.Relu,
                                     bias=b1_sb[:, m:m + 1]).then_inc(h1_made, 1)
            act.wait_ge(h2_summed, 1)
            nc.scalar.activation(h2_sb[:, 0, :], t_ps[:, 2, 0, :], ACT.Relu,
                                 bias=b2_sb[:, 0:1]).then_inc(h2_made, 1)
            act.wait_ge(y_summed, 1)
            nc.scalar.activation(y_sb[:], f_ps[0:1, :], ACT.Copy).then_inc(y_made, 1)

        @block.vector
        def _(dve):
            nc.vector.memset(ident[:], 0.0).then_inc(zeroed, 1)
            nc.vector.memset(ones_at[:], 0.0).then_inc(zeroed, 1)
            dve.wait_ge(zeroed, 2)
            nc.vector.memset(ones_at[0:64, 30:31], 1.0).then_inc(consts_made, 1)
            nc.vector.memset(ones_at[64:128, 31:32], 1.0).then_inc(consts_made, 1)

            def rest_of_x(k):
                s = k % X_SLOTS
                dve.wait_ge(f_copied, 2 * (k + 1))
                if k >= X_SLOTS:
                    dve.wait_ge(xl_placed[s], 64 * (k // X_SLOTS))
                nc.vector.tensor_tensor(feat_lo[:, s, :], feat[:, k, :], feat_hi[:, s, :].bitcast(F32),
                                        ALU.subtract).then_inc(fl_made, 1)

            def rest_of_k(q):
                s = q % H_SLOTS
                dve.wait_ge(kh_made, q + 1)
                if q >= H_SLOTS:
                    n = q - H_SLOTS
                    dve.wait_ge(kl_placed[n % S_SLOTS], 32 * (n // S_SLOTS + 1))
                nc.vector.tensor_tensor(k_lo[:, s, :], k_raw[:, q % R_SLOTS, :], k_hi[:, s, :].bitcast(F32),
                                        ALU.subtract).then_inc(kl_made, 1)

            def make_z(n):
                dve.wait_ge(summed, ZT // BATCH_T * (n + 1))
                if n == 0:
                    dve.wait_ge(w_loaded, 16 * W_DMAS)
                nc.vector.tensor_tensor(z_sb[:, n, :], z_ps[:], dense_sb[:, n, :],
                                        ALU.add).then_inc(z_made, 1)

            events = [(turn(k) + (2 if k > 7 else 0), 1, rest_of_x, k) for k in range(NK)]
            events += [(split_turn(q) + 2, 0, rest_of_k, q) for q in range(NQ)]
            events += [(ZT * (n + 1) + 4, 2, make_z, n) for n in range(NZ)]
            events.sort(key=lambda x: (x[0], x[1], x[3]))
            for g, (k, j) in enumerate(GROUPS):
                while events and events[0][0] <= FIRST_TILE[g]:
                    _, _, step, n = events.pop(0)
                    step(n)
                dve.wait_ge(t_made, g + 1)
                if g >= P_SLOTS:
                    last = FIRST_TILE[g - P_SLOTS + 1] - 1
                    dve.wait_ge(summed, last // BATCH_T + 1)
                n = len(GROUP_C[g])
                nc.vector.tensor_tensor(
                    prod[:, g % P_SLOTS, 0:n, :], t_ps[:, g % T_SLOTS, 0:n, :],
                    feat[:, j:j + 1, :].broadcast_to([P, n, BATCH]), ALU.mult).then_inc(p_made, 1)
            for _, _, step, n in events:
                step(n)
            for m in range(1, M1, 2):
                dve.wait_ge(h1_summed, m + 1)
                nc.vector.tensor_scalar(h1_sb[:, m, :], t_ps[:, m // 2, m % 2, :], b1_sb[:, m:m + 1], 0.0,
                                        ALU.add, ALU.max).then_inc(h1_made, 1)
            dve.wait_ge(h2_summed, 2)
            nc.vector.tensor_scalar(h2_sb[:, 1, :], t_ps[:, 2, 1, :], b2_sb[:, 1:2], 0.0,
                                    ALU.add, ALU.max).then_inc(h2_made, 1)

        @block.tensor
        def _(pe):
            def transpose_fields(k):
                if k == 0:
                    pe.wait_ge(consts_made, 3)
                pe.wait_ge(gathered[k % E_SLOTS], 128 * (k // E_SLOTS + 1))
                if k > 0:
                    pe.wait_ge(xh_placed, 4 * k)
                for t in range(BT):
                    last = nc.tensor.transpose(f_ps[:, P * t:P * (t + 1)], emb[:, k % E_SLOTS, t, :],
                                               ident[:])
                last.then_inc(f_transposed, 1)

            def contract(g):
                k, j = GROUPS[g]
                if j == 0:
                    pe.wait_ge(xh_placed, 4 * (k + 1))
                    pe.wait_ge(xl_placed[k % X_SLOTS], 64 * (k // X_SLOTS + 1))
                if g >= T_SLOTS:
                    pe.wait_ge(p_made, g - T_SLOTS + 1)
                for i, c in enumerate(GROUP_C[g]):
                    t = FIRST_TILE[g] + i
                    q = t // CHUNK
                    if t % CHUNK == 0:
                        pe.wait_ge(kh_placed, 2 * (q + 1))
                        pe.wait_ge(kl_placed[q % S_SLOTS], 32 * (q // S_SLOTS + 1))
                    b = t % CHUNK // 2
                    weights = k_st[:, q % S_SLOTS, t % 2, P * b:P * (b + 1)]
                    nc.tensor.matmul(t_ps[:, g % T_SLOTS, i, :], weights, x_hi[:, k % X_SLOTS, c % 2, :],
                                     start=True, stop=False)
                    last = nc.tensor.matmul(t_ps[:, g % T_SLOTS, i, :], weights, x_lo[:, k % X_SLOTS, c % 2, :],
                                            start=False, stop=True)
                last.then_inc(t_made, 1)

            def sum_batch(m):
                t0 = BATCH_T * m
                n, at = t0 // ZT, t0 % ZT // BATCH_T
                pe.wait_ge(p_made, TILES[t0 + BATCH_T - 1][0] + 1)
                if at == 0 and n > 0:
                    pe.wait_ge(z_made, n)
                for t in range(t0, t0 + BATCH_T):
                    g, i, _, _ = TILES[t]
                    a = 32 * (t % BATCH_T)
                    last = nc.tensor.matmul(z_ps[a:a + 32, :], ones_at[:, 30 - 2 * at:62 - 2 * at],
                                            prod[:, g % P_SLOTS, i, :], start=(at == 0),
                                            stop=(at == ZT // BATCH_T - 1), tile_position=(0, a))
                last.then_inc(summed, 1)

            turns = [(turn(k), k) for k in range(NK)]
            m = 0
            for g in range(len(GROUPS)):
                while turns and turns[0][0] <= FIRST_TILE[g]:
                    transpose_fields(turns.pop(0)[1])
                contract(g)
                while m < NT // BATCH_T and (TILES[BATCH_T * (m + 1) - 1][0]
                                             <= g - SUM_LAG - Z_LAG * (m * BATCH_T % ZT == 0)):
                    sum_batch(m)
                    m += 1
            while BATCH_T * m < NT:
                sum_batch(m)
                m += 1

            pe.wait_ge(w_loaded, 16 * W_DMAS)
            pe.wait_ge(p_made, len(GROUPS))
            for n in range(NZ):
                pe.wait_ge(z_made, n + 1)
                for i in range(M1):
                    last = nc.tensor.matmul(t_ps[:, i // 2, i % 2, :], w1_sb[:, n, P * i:P * (i + 1)],
                                            z_sb[:, n, :], start=(n == 0), stop=(n == NZ - 1))
                    if n == NZ - 1:
                        last.then_inc(h1_summed, 1)
            pe.wait_ge(h1_made, M1)
            for m in range(M2):
                for i in range(M1):
                    last = nc.tensor.matmul(t_ps[:, 2, m, :], w2_sb[:, i, P * m:P * (m + 1)], h1_sb[:, i, :],
                                            start=(i == 0), stop=(i == M1 - 1))
                last.then_inc(h2_summed, 1)
            pe.wait_ge(h2_made, M2)
            for m in range(M2):
                last = nc.tensor.matmul(f_ps[0:1, :], w3_sb[:, m:m + 1], h2_sb[:, m, :],
                                        start=(m == 0), stop=(m == M2 - 1))
            last.then_inc(y_summed, 1)


def kernel(**inputs):
    import concourse.bacc as bacc
    from concourse.bass_utils import run_bass_kernel_spmd

    pair_at = {rc: n for n, rc in enumerate(zip(*np.triu_indices(FIELDS, k=1)))}
    k_in = np.asarray(inputs["L0_rec_kernel"])
    w1_in = np.asarray(inputs["W_top1"])
    dense_in = np.asarray(inputs["dense_ctx"])
    n_pairs = k_in.shape[1]
    k_tiles = np.zeros((NQ, 2, EMBED, BLOCKS, 2, EMBED), k_in.dtype)
    w1 = np.zeros((P, NZ, HID1), w1_in.dtype)
    dense_z = np.zeros((P, NZ, BATCH), dense_in.dtype)
    free = 0
    for t in range(NT):
        for i, rc in enumerate(tile_fields(t)):
            n, row = z_row(t, i)
            if rc in pair_at:
                k_tiles[t // CHUNK, t % 2, :, t % CHUNK // 2, i, :] = k_in[:, pair_at[rc], :]
                w1[row, n] = w1_in[pair_at[rc]]
            else:
                w1[row, n] = w1_in[n_pairs + free]
                dense_z[row, n] = dense_in[:, free]
                free += 1

    arrays = {
        "dense_z": dense_z,
        "ids": np.ascontiguousarray(inputs["ids"]),
        **{f"tbl_{f}": np.ascontiguousarray(inputs[f"tbl_{f}"]) for f in range(FIELDS)},
        "k_tiles": k_tiles.reshape(NQ, P, CC),
        "w1": w1,
        "w2": np.ascontiguousarray(np.asarray(inputs["W_top2"]).reshape(M1, P, HID2).transpose(1, 0, 2)),
        "w3": np.ascontiguousarray(np.asarray(inputs["W_top3"]).reshape(M2, P).T),
        "b1": np.ascontiguousarray(np.asarray(inputs["b_top1"]).reshape(M1, P).T),
        "b2": np.ascontiguousarray(np.asarray(inputs["b_top2"]).reshape(M2, P).T),
    }
    nc = bacc.Bacc("TRN2", target_bir_lowering=False, num_devices=1)
    ap = {n: nc.dram_tensor(n, a.shape, mybir.dt.from_np(a.dtype), kind="ExternalInput").ap()
          for n, a in arrays.items()}
    y = nc.dram_tensor("y", (BATCH, 1), F32, kind="ExternalOutput").ap()
    dlrm_tower(nc, ap["dense_z"], ap["ids"], [ap[f"tbl_{f}"] for f in range(FIELDS)], ap["k_tiles"],
               ap["w1"], ap["w2"], ap["w3"], ap["b1"], ap["b2"], y)
    return run_bass_kernel_spmd(nc, [arrays], core_ids=[0]).results[0]["y"]
```

```python
from contextlib import ExitStack

import numpy as np

import concourse.bass as bass
from concourse import mybir

F32 = mybir.dt.float32
F32R = mybir.dt.float32r
BF16 = mybir.dt.bfloat16
I32 = mybir.dt.int32
I16 = mybir.dt.int16
ALU = mybir.AluOpType
ACT = mybir.ActivationFunctionType

P = 128
FIELDS = 32
EMBED = 64
BATCH = 512
BT = BATCH // P
NK = FIELDS // 2
HID1, HID2 = 512, 256
M1, M2 = HID1 // P, HID2 // P

GROUPS = [(k, j) for k in range(NK) for j in range(k + 1)]
GROUP_C = [[2 * k, 2 * k + 1] if j < k else [2 * k + 1] for k, j in GROUPS]
TILES = [(g, i, c, GROUPS[g][1]) for g, cs in enumerate(GROUP_C) for i, c in enumerate(cs)]
FIRST_TILE = [next(t for t, x in enumerate(TILES) if x[0] == g) for g in range(len(GROUPS))]
NT = len(TILES)
GROUP_END = [sum(k + 1 for k in range(n + 1)) for n in range(NK)]

CHUNK = 16
BLOCKS = CHUNK // 2
NQ = NT // CHUNK
CC = BLOCKS * P

ZT = 64
NZ = NT // ZT
BATCH_T = 4

LOOKED_UP = [0, 3]
LOOKUP_TURN = [-20, -10]
GATHERED = [k for k in range(NK) if k not in LOOKED_UP]
TP = 125
PARTS = 3

E_SLOTS, X_SLOTS, R_SLOTS, H_SLOTS, S_SLOTS, T_SLOTS, P_SLOTS = 3, 3, 3, 2, 4, 3, 8
SUM_LAG = 3
Z_LAG = 1
X_LEAD = 13


def z_row(t, i):
    return t // ZT, 32 * (t % BATCH_T) + 2 * ((t % ZT) // BATCH_T) + i


def tile_fields(t):
    _, _, c, j = TILES[t]
    return [(2 * j, c), (2 * j + 1, c)]


def turn(k):
    return (0, 0, 0, 1, 6)[k] if k < 5 else max((k - 2) ** 2, k * k - X_LEAD)


def split_turn(q):
    return (-16, 2, 7, 15)[q] if q < S_SLOTS else CHUNK * (q - S_SLOTS + 1) + 1


def dlrm_tower(nc, dense_z, ids, ids_up, minus_first_row, tables, k_tiles, w1, w2, w3, b1, b2, out):
    rows = {f: tables[f].shape[0] // TP for k in LOOKED_UP for f in (2 * k, 2 * k + 1)}
    max_rows = max(rows.values())
    assert all(rows[f] * TP == tables[f].shape[0] for f in rows)
    lookups = {k: [(i, r) for r in range(max_rows) for i in range(2) if r < rows[2 * k + i]] for k in LOOKED_UP}
    first_lookup = {k: sum(len(lookups[n]) for n in LOOKED_UP if n < k) for k in LOOKED_UP}

    ctx = ExitStack()
    with ctx:
        def sb(name, shape, dt=F32):
            return ctx.enter_context(nc.sbuf_tensor(name, shape, dt))

        def ps(name, shape):
            return ctx.enter_context(nc.psum_tensor(name, shape, F32))

        def sem(name):
            return ctx.enter_context(nc.semaphore(name))

        def upper_half(ap):
            return ap[:].bitcast(BF16).rearrange("p i (w t) -> p i w t", t=2)[:, :, :, 1]

        ids_sb = sb("ids_sb", [P, BT, FIELDS], I32)
        emb = sb("emb", [P, E_SLOTS, BT, 2 * EMBED])
        rest = [sb(f"rest{n}", [TP, 2, max_rows * EMBED]) for n in range(len(LOOKED_UP))]
        part3 = [sb(f"part3_{n}", [TP, 2, max_rows * EMBED], BF16) for n in range(len(LOOKED_UP))]
        ids_short = sb("ids_short", [TP, len(rows), BATCH], I16)
        minus_first_row_sb = sb("minus_first_row_sb", [TP, len(rows)])
        ident = sb("ident", [P, P])
        zeros = sb("zeros", [P, BATCH], BF16)
        ones_at = sb("ones_at", [P, 62])
        feat = sb("feat", [P, NK, BATCH])
        feat_hi = sb("feat_hi", [P, 2, BATCH], F32R)
        feat_lo = sb("feat_lo", [P, 2, BATCH], F32R)
        x_hi = sb("x_hi", [P, X_SLOTS, 2, BATCH], F32R)
        x_lo = sb("x_lo", [P, X_SLOTS, 2, BATCH], F32R)
        k_raw = sb("k_raw", [P, R_SLOTS, CC])
        k_hi = sb("k_hi", [P, H_SLOTS, CC], F32R)
        k_lo = sb("k_lo", [P, H_SLOTS, CC], F32R)
        k_st = sb("k_st", [P, S_SLOTS, 2, CC], F32R)
        prod = sb("prod", [P, P_SLOTS, 2, BATCH])
        z_sb = sb("z_sb", [P, NZ, BATCH])
        table = [prod[0:TP, P_SLOTS - 2:P_SLOTS, :, :].rearrange("p a b n -> p (a b n)"),
                 z_sb[0:TP, :, :].rearrange("p a n -> p (a n)")]
        table = [t[:, 0:2 * max_rows * EMBED].rearrange("p (i w) -> p i w", i=2) for t in table]
        one_hot = [prod[0:TP, 0:max_rows // 2, :, :].bitcast(BF16).rearrange("p a c (b n) -> p (a c b) n", b=2),
                   feat[0:TP, NK - max_rows:NK, :].bitcast(BF16).rearrange("p a (b n) -> p (a b) n", b=2)]
        w1_sb = sb("w1_sb", [P, NZ, HID1])
        ids_wide = w1_sb[:].bitcast(I32)
        parts = [[upper_half(table[n]), upper_half(rest[n]), part3[n]] for n in range(len(LOOKED_UP))]
        w2_sb = sb("w2_sb", [P, M1, HID2])
        w3_sb = sb("w3_sb", [P, M2])
        b1_sb = sb("b1_sb", [P, M1])
        b2_sb = sb("b2_sb", [P, M2])
        h1_sb = prod[:, 0:2, :, :].rearrange("p a b n -> p (a b) n")
        h2_sb = prod[:, 2, :, :]
        y_sb = sb("y_sb", [1, BATCH])

        t_ps = ps("t_ps", [P, T_SLOTS, 2, BATCH])
        z_ps = ps("z_ps", [P, BATCH])
        f_ps = ps("f_ps", [P, BATCH])

        ids_loaded = sem("ids_loaded")
        minus_first_row_loaded = sem("minus_first_row_loaded")
        consts_made = sem("consts_made")
        zeros_made = sem("zeros_made")
        zeroed = sem("zeroed")
        ids_wide_loaded = [sem(f"ids_wide_loaded{i}") for i in range(len(LOOKED_UP))]
        ids_short_made = sem("ids_short_made")
        tables_loaded = [sem(f"tables_loaded{i}") for i in range(len(LOOKED_UP))]
        rest_made = sem("rest_made")
        part3_made = sem("part3_made")
        one_hot_made = sem("one_hot_made")
        gathered = [sem(f"gathered{i}") for i in range(E_SLOTS)]
        f_transposed = sem("f_transposed")
        f_copied = sem("f_copied")
        fl_made = sem("fl_made")
        xh_placed = sem("xh_placed")
        xl_placed = [sem(f"xl_placed{i}") for i in range(X_SLOTS)]
        k_loaded = [sem(f"k_loaded{i}") for i in range(R_SLOTS)]
        kh_made = sem("kh_made")
        kh_placed = sem("kh_placed")
        kl_made = sem("kl_made")
        kl_placed = [sem(f"kl_placed{i}") for i in range(S_SLOTS)]
        t_made = sem("t_made")
        p_made = sem("p_made")
        summed = sem("summed")
        z_made = sem("z_made")
        dense_loaded = sem("dense_loaded")
        w_loaded = sem("w_loaded")
        h1_summed = sem("h1_summed")
        h1_made = sem("h1_made")
        h2_summed = sem("h2_summed")
        h2_made = sem("h2_made")
        y_summed = sem("y_summed")
        y_made = sem("y_made")
        y_stored = sem("y_stored")

        W_DMAS = NZ + 4

        def tiles_gone(eng, t):
            if t > 0:
                eng.wait_ge(t_made, TILES[t - 1][0] + 1)

        def fields_at(k):
            return t_ps[:, 2, 1, :] if k == LOOKED_UP[0] else z_ps[:] if k == LOOKED_UP[1] else f_ps[:]

        def x_slot_free(eng, k):
            if k >= X_SLOTS:
                eng.wait_ge(t_made, GROUP_END[k - X_SLOTS])

        block = ctx.enter_context(nc.Block())

        @block.sync
        def _(sp):
            sp.dma_start(minus_first_row_sb[:], minus_first_row).then_inc(minus_first_row_loaded, 16)
            sp.dma_start(ids_sb[:], ids.rearrange("(t p) f -> p t f", p=P)).then_inc(ids_loaded, 16)

            def load_tables(k):
                n = LOOKED_UP.index(k)
                for i in range(2):
                    f = 2 * k + i
                    sp.dma_start(table[n][:, i, 0:rows[f] * EMBED],
                                 tables[f].rearrange("(p r) e -> p (r e)", p=TP)).then_inc(tables_loaded[n], 16)
                sp.dma_start(ids_wide[:, 2 * n:2 * n + 2, :], ids_up[:, 2 * n:2 * n + 2, :].broadcast_to(
                    [P, 2, BATCH])).then_inc(ids_wide_loaded[n], 16)

            def load_k(q):
                if q >= R_SLOTS:
                    sp.wait_ge(kl_made, q - R_SLOTS + 1)
                    sp.wait_ge(kh_placed, 2 * (q - R_SLOTS + 1))
                sp.dma_start(k_raw[:, q % R_SLOTS, :], k_tiles[q]).then_inc(k_loaded[q % R_SLOTS], 16)

            def place_k_lo(q):
                sp.wait_ge(kl_made, q + 1)
                tiles_gone(sp, CHUNK * (q - S_SLOTS + 1))
                s, r = q % S_SLOTS, q % H_SLOTS
                for side, to, of in ((0, slice(64, 128), slice(0, 64)), (1, slice(0, 64), slice(64, 128))):
                    sp.dma_start(k_st[to, s, side, :].bitcast(F32),
                                 k_lo[of, r, :].bitcast(F32)).then_inc(kl_placed[s], 16)

            def place_x_lo(k):
                sp.wait_ge(fl_made, k + 1)
                x_slot_free(sp, k)
                s = k % X_SLOTS
                for i in range(2):
                    for to in (slice(0, 64), slice(64, 128)):
                        sp.dma_start(x_lo[to, s, i, :].bitcast(F32),
                                     feat_lo[64 * i:64 * i + 64, k % 2, :].bitcast(F32)).then_inc(xl_placed[s], 16)

            weights = [(to[:, n, :], of[:, n, :], loaded) for to, of, loaded in
                       ((z_sb, dense_z, dense_loaded), (w1_sb, w1, w_loaded)) for n in range(NZ)]
            weights += [(to[:], of, w_loaded) for to, of in ((w2_sb, w2), (w3_sb, w3), (b1_sb, b1), (b2_sb, b2))]

            def load_weights():
                if len(weights) == 2 * NZ + 4:
                    sp.wait_ge(ids_short_made, len(rows))
                    sp.wait_ge(f_transposed, LOOKED_UP[1] + 1)
                for to, of, loaded in weights[:2]:
                    sp.dma_start(to, of).then_inc(loaded, 16)
                del weights[:2]

            events = [(turn(k) + (2 if k > 7 else 0), 2, place_x_lo, k) for k in range(NK)]
            events += [(split_turn(q) + 2.5, 1, place_k_lo, q) for q in range(NQ)]
            events += [(-110, 0, load_tables, k) for k in LOOKED_UP]
            events += [(-100 if q == 0 else -12 if q < R_SLOTS else max(split_turn(q - R_SLOTS) + 4, 1), 0, load_k, q)
                       for q in range(NQ)]
            for _, _, step, n in sorted(events, key=lambda x: (x[0], x[1], x[3])):
                step(n)
                if step is place_x_lo and n >= 6:
                    load_weights()
            sp.wait_ge(y_made, 1)
            sp.dma_start(out.rearrange("b o -> o b"), y_sb[:]).then_inc(y_stored, 16)
            sp.wait_ge(y_stored, 16)

        @block.gpsimd
        def _(pool):
            pool.wait_ge(zeroed, 1)
            nc.gpsimd.affine_select(out=ident[:], in_=ident[:], compare_op=ALU.not_equal, fill=1.0,
                                    base=0, pattern=[[-1, P]], channel_multiplier=1).then_inc(consts_made, 1)
            pool.wait_ge(ids_loaded, 16)
            for n, k in enumerate(GATHERED):
                if n >= E_SLOTS:
                    pool.wait_ge(f_transposed, GATHERED[n - E_SLOTS] + 1)
                for i in range(2):
                    for t in range(BT):
                        f = 2 * k + i
                        pool.indirect_dma_start(
                            emb[:, n % E_SLOTS, t, EMBED * i:EMBED * (i + 1)], None, tables[f],
                            bass.IndirectOffsetOnAxis(ap=ids_sb[:, t, f:f + 1], axis=0),
                        ).then_inc(gathered[n % E_SLOTS], 16)

        @block.scalar
        def _(act):
            def split_x(k):
                s = k % X_SLOTS
                act.wait_ge(f_transposed, k + 1)
                if k >= 2:
                    act.wait_ge(fl_made, k - 1)
                nc.scalar.activation(feat_hi[:, k % 2, :], fields_at(k), ACT.Copy).then_inc(f_copied, 1)
                nc.scalar.activation(feat[:, k, :], fields_at(k), ACT.Copy).then_inc(f_copied, 1)
                x_slot_free(act, k)
                for i in range(2):
                    for to in (slice(0, 64), slice(64, 128)):
                        nc.scalar.activation(x_hi[to, s, i, :], fields_at(k)[64 * i:64 * i + 64, :],
                                             ACT.Copy).then_inc(xh_placed, 1)

            def split_k(q):
                raw = k_raw[:, q % R_SLOTS, :]
                act.wait_ge(k_loaded[q % R_SLOTS], 16 * (q // R_SLOTS + 1))
                if q >= H_SLOTS:
                    act.wait_ge(kl_made, q - H_SLOTS + 1)
                nc.scalar.activation(k_hi[:, q % H_SLOTS, :], raw, ACT.Copy).then_inc(kh_made, 1)
                tiles_gone(act, CHUNK * (q - S_SLOTS + 1))
                for side, at in ((0, slice(0, 64)), (1, slice(64, 128))):
                    nc.scalar.activation(k_st[at, q % S_SLOTS, side, :], raw[at, :],
                                         ACT.Copy).then_inc(kh_placed, 1)

            def shorten_ids(k):
                n = LOOKED_UP.index(k)
                act.wait_ge(ids_wide_loaded[n], 16)
                if n == 0:
                    act.wait_ge(minus_first_row_loaded, 16)
                for at in (2 * n, 2 * n + 1):
                    nc.scalar.activation(ids_short[:, at, :], ids_wide[0:TP, at, :], ACT.Identity,
                                         bias=minus_first_row_sb[:, at:at + 1]).then_inc(ids_short_made, 1)

            for k in LOOKED_UP:
                shorten_ids(k)
            events = [(turn(k), 1, split_x, k) for k in range(NK)]
            events += [(split_turn(q), 0, split_k, q) for q in range(NQ)]
            for _, _, step, n in sorted(events, key=lambda x: (x[0], x[1], x[3])):
                step(n)
            act.wait_ge(w_loaded, 16 * W_DMAS)
            for m in range(0, M1, 2):
                act.wait_ge(h1_summed, m + 1)
                nc.scalar.activation(h1_sb[:, m, :], t_ps[:, m // 2, m % 2, :], ACT.Relu,
                                     bias=b1_sb[:, m:m + 1]).then_inc(h1_made, 1)
            act.wait_ge(h2_summed, 1)
            nc.scalar.activation(h2_sb[:, 0, :], t_ps[:, 2, 0, :], ACT.Relu,
                                 bias=b2_sb[:, 0:1]).then_inc(h2_made, 1)
            act.wait_ge(y_summed, 1)
            nc.scalar.activation(y_sb[:], f_ps[0:1, :], ACT.Copy).then_inc(y_made, 1)

        @block.vector
        def _(dve):
            nc.vector.memset(zeros[:], 0.0).then_inc(zeros_made, 1)
            nc.vector.memset(ident[:], 0.0).then_inc(zeroed, 1)
            nc.vector.memset(ones_at[:], 0.0).then_inc(zeroed, 1)
            dve.wait_ge(zeroed, 2)
            nc.vector.memset(ones_at[0:64, 30:31], 1.0).then_inc(consts_made, 1)
            nc.vector.memset(ones_at[64:128, 31:32], 1.0).then_inc(consts_made, 1)

            def rest_of_x(k):
                dve.wait_ge(f_copied, 2 * (k + 1))
                if k >= 2:
                    dve.wait_ge(xl_placed[(k - 2) % X_SLOTS], 64 * ((k - 2) // X_SLOTS + 1))
                nc.vector.tensor_tensor(feat_lo[:, k % 2, :], feat[:, k, :], feat_hi[:, k % 2, :].bitcast(F32),
                                        ALU.subtract).then_inc(fl_made, 1)

            def rest_of_k(q):
                s = q % H_SLOTS
                dve.wait_ge(kh_made, q + 1)
                if q >= H_SLOTS:
                    n = q - H_SLOTS
                    dve.wait_ge(kl_placed[n % S_SLOTS], 32 * (n // S_SLOTS + 1))
                nc.vector.tensor_tensor(k_lo[:, s, :], k_raw[:, q % R_SLOTS, :], k_hi[:, s, :].bitcast(F32),
                                        ALU.subtract).then_inc(kl_made, 1)

            def split_tables(k):
                n = LOOKED_UP.index(k)
                dve.wait_ge(tables_loaded[n], 32)
                for i in range(2):
                    w = rows[2 * k + i] * EMBED
                    nc.vector.tensor_tensor(rest[n][:, i, 0:w], table[n][:, i, 0:w], parts[n][0][:, i, 0:w],
                                            ALU.subtract).then_inc(rest_made, 1)
                for i in range(2):
                    w = rows[2 * k + i] * EMBED
                    dve.wait_ge(rest_made, 2 * n + i + 1)
                    nc.vector.tensor_tensor(part3[n][:, i, 0:w], rest[n][:, i, 0:w], parts[n][1][:, i, 0:w],
                                            ALU.subtract).then_inc(part3_made, 1)

            def make_one_hots(k, which=slice(0, 10)):
                n = LOOKED_UP.index(k)
                dve.wait_ge(ids_short_made, 2 * (n + 1))
                for at, (i, r) in list(enumerate(lookups[k]))[which]:
                    nc.vector.tensor_scalar(one_hot[n][:, at, :], ids_short[:, 2 * n + i, :], float(r), None,
                                            ALU.is_equal).then_inc(one_hot_made, 1)

            def rest_of_one_hots(k):
                make_one_hots(k, slice(10, None))

            def make_z(n):
                dve.wait_ge(summed, ZT // BATCH_T * (n + 1))
                if n == 0:
                    dve.wait_ge(dense_loaded, 16 * NZ)
                nc.vector.tensor_tensor(z_sb[:, n, :], z_ps[:], z_sb[:, n, :],
                                        ALU.add).then_inc(z_made, 1)

            events = [(LOOKUP_TURN[1] + 1.5 if k == 0 else turn(k) + (2 if k > 7 else 0), 1, rest_of_x, k)
                      for k in range(NK)]
            events += [(split_turn(q) + 2, 0, rest_of_k, q) for q in range(NQ)]
            events += [(ZT * (n + 1) + 6, 2, make_z, n) for n in range(NZ)]
            for n, k in enumerate(LOOKED_UP):
                events += [(LOOKUP_TURN[n], 3, split_tables, k), (LOOKUP_TURN[n] + 1, 3, make_one_hots, k),
                           (LOOKUP_TURN[n] + 2, 3, rest_of_one_hots, k)]
            events.sort(key=lambda x: (x[0], x[1], x[3]))
            for g, (k, j) in enumerate(GROUPS):
                while events and events[0][0] <= FIRST_TILE[g]:
                    _, _, step, n = events.pop(0)
                    step(n)
                dve.wait_ge(t_made, g + 1)
                if g >= P_SLOTS:
                    last = FIRST_TILE[g - P_SLOTS + 1] - 1
                    dve.wait_ge(summed, last // BATCH_T + 1)
                n = len(GROUP_C[g])
                nc.vector.tensor_tensor(
                    prod[:, g % P_SLOTS, 0:n, :], t_ps[:, g % T_SLOTS, 0:n, :],
                    feat[:, j:j + 1, :].broadcast_to([P, n, BATCH]), ALU.mult).then_inc(p_made, 1)
            for _, _, step, n in events:
                step(n)
            dve.wait_ge(w_loaded, 16 * W_DMAS)
            for m in range(1, M1, 2):
                dve.wait_ge(h1_summed, m + 1)
                nc.vector.tensor_scalar(h1_sb[:, m, :], t_ps[:, m // 2, m % 2, :], b1_sb[:, m:m + 1], 0.0,
                                        ALU.add, ALU.max).then_inc(h1_made, 1)
            dve.wait_ge(h2_summed, 2)
            nc.vector.tensor_scalar(h2_sb[:, 1, :], t_ps[:, 2, 1, :], b2_sb[:, 1:2], 0.0,
                                    ALU.add, ALU.max).then_inc(h2_made, 1)

        @block.tensor
        def _(pe):
            def keep_warm(count):
                for _ in range(count):
                    nc.tensor.matmul(z_ps[:], zeros[:, 0:P], zeros[:], start=True, stop=True)

            def look_up_fields(k, first, end):
                n = LOOKED_UP.index(k)
                if first == 0:
                    keep_warm(18 if n == 0 else 5)
                    pe.wait_ge(part3_made, 2 * (n + 1))
                for r, part in ((r, part) for r in range(first, end) for part in range(PARTS)):
                    pair = [at for at, x in enumerate(lookups[k]) if x[1] == r]
                    if part == 0:
                        pe.wait_ge(one_hot_made, first_lookup[k] + pair[-1] + 1)
                    for at in pair:
                        i = lookups[k][at][0]
                        last = nc.tensor.matmul(
                            fields_at(k)[EMBED * i:EMBED * (i + 1), :],
                            parts[n][part][:, i, EMBED * r:EMBED * (r + 1)],
                            one_hot[n][:, at, :], start=(r == 0 and part == 0),
                            stop=(r == rows[2 * k + i] - 1 and part == PARTS - 1),
                            tile_position=(0, EMBED * i))
                if end == max_rows:
                    last.then_inc(f_transposed, 1)

            def transpose_fields(k):
                n = GATHERED.index(k)
                if n == 0:
                    pe.wait_ge(consts_made, 3)
                pe.wait_ge(gathered[n % E_SLOTS], 128 * (n // E_SLOTS + 1))
                if n > 0:
                    pe.wait_ge(xh_placed, 4 * (GATHERED[n - 1] + 1))
                for t in range(BT):
                    last = nc.tensor.transpose(f_ps[:, P * t:P * (t + 1)], emb[:, n % E_SLOTS, t, :],
                                               ident[:])
                last.then_inc(f_transposed, 1)

            def contract(g):
                k, j = GROUPS[g]
                if j == 0:
                    pe.wait_ge(xh_placed, 4 * (k + 1))
                    pe.wait_ge(xl_placed[k % X_SLOTS], 64 * (k // X_SLOTS + 1))
                if g >= T_SLOTS:
                    pe.wait_ge(p_made, g - T_SLOTS + 1)
                for i, c in enumerate(GROUP_C[g]):
                    t = FIRST_TILE[g] + i
                    q = t // CHUNK
                    if t % CHUNK == 0:
                        pe.wait_ge(kh_placed, 2 * (q + 1))
                        pe.wait_ge(kl_placed[q % S_SLOTS], 32 * (q // S_SLOTS + 1))
                    b = t % CHUNK // 2
                    weights = k_st[:, q % S_SLOTS, t % 2, P * b:P * (b + 1)]
                    nc.tensor.matmul(t_ps[:, g % T_SLOTS, i, :], weights, x_hi[:, k % X_SLOTS, c % 2, :],
                                     start=True, stop=False)
                    last = nc.tensor.matmul(t_ps[:, g % T_SLOTS, i, :], weights, x_lo[:, k % X_SLOTS, c % 2, :],
                                            start=False, stop=True)
                last.then_inc(t_made, 1)

            def sum_batch(m):
                t0 = BATCH_T * m
                n, at = t0 // ZT, t0 % ZT // BATCH_T
                pe.wait_ge(p_made, TILES[t0 + BATCH_T - 1][0] + 1)
                if at == 0 and n > 0:
                    pe.wait_ge(z_made, n)
                for t in range(t0, t0 + BATCH_T):
                    g, i, _, _ = TILES[t]
                    a = 32 * (t % BATCH_T)
                    last = nc.tensor.matmul(z_ps[a:a + 32, :], ones_at[:, 30 - 2 * at:62 - 2 * at],
                                            prod[:, g % P_SLOTS, i, :], start=(at == 0),
                                            stop=(at == ZT // BATCH_T - 1), tile_position=(0, a))
                last.then_inc(summed, 1)

            pe.wait_ge(zeros_made, 1)
            look_up_fields(LOOKED_UP[0], 0, max_rows)
            transpose_fields(1)
            look_up_fields(LOOKED_UP[1], 0, 7)
            transpose_fields(2)
            look_up_fields(LOOKED_UP[1], 7, max_rows)
            later = list(range(4, NK))
            m = 0
            for g in range(len(GROUPS)):
                while later and turn(later[0]) <= FIRST_TILE[g]:
                    transpose_fields(later.pop(0))
                contract(g)
                while m < NT // BATCH_T and (TILES[BATCH_T * (m + 1) - 1][0]
                                             <= g - SUM_LAG - Z_LAG * (m * BATCH_T % ZT == 0)):
                    sum_batch(m)
                    m += 1
            while BATCH_T * m < NT:
                sum_batch(m)
                m += 1

            pe.wait_ge(w_loaded, 16 * W_DMAS)
            pe.wait_ge(p_made, len(GROUPS))
            for n in range(NZ):
                pe.wait_ge(z_made, n + 1)
                for i in range(M1):
                    last = nc.tensor.matmul(t_ps[:, i // 2, i % 2, :], w1_sb[:, n, P * i:P * (i + 1)],
                                            z_sb[:, n, :], start=(n == 0), stop=(n == NZ - 1))
                    if n == NZ - 1:
                        last.then_inc(h1_summed, 1)
            pe.wait_ge(h1_made, M1)
            for m in range(M2):
                for i in range(M1):
                    last = nc.tensor.matmul(t_ps[:, 2, m, :], w2_sb[:, i, P * m:P * (m + 1)], h1_sb[:, i, :],
                                            start=(i == 0), stop=(i == M1 - 1))
                last.then_inc(h2_summed, 1)
            pe.wait_ge(h2_made, M2)
            for m in range(M2):
                last = nc.tensor.matmul(f_ps[0:1, :], w3_sb[:, m:m + 1], h2_sb[:, m, :],
                                        start=(m == 0), stop=(m == M2 - 1))
            last.then_inc(y_summed, 1)


def kernel(**inputs):
    import concourse.bacc as bacc
    from concourse.bass_utils import run_bass_kernel_spmd

    pair_at = {rc: n for n, rc in enumerate(zip(*np.triu_indices(FIELDS, k=1)))}
    k_in = np.asarray(inputs["L0_rec_kernel"])
    w1_in = np.asarray(inputs["W_top1"])
    dense_in = np.asarray(inputs["dense_ctx"])
    n_pairs = k_in.shape[1]
    k_tiles = np.zeros((NQ, 2, EMBED, BLOCKS, 2, EMBED), k_in.dtype)
    w1 = np.zeros((P, NZ, HID1), w1_in.dtype)
    dense_z = np.zeros((P, NZ, BATCH), dense_in.dtype)
    free = 0
    for t in range(NT):
        for i, rc in enumerate(tile_fields(t)):
            n, row = z_row(t, i)
            if rc in pair_at:
                k_tiles[t // CHUNK, t % 2, :, t % CHUNK // 2, i, :] = k_in[:, pair_at[rc], :]
                w1[row, n] = w1_in[pair_at[rc]]
            else:
                w1[row, n] = w1_in[n_pairs + free]
                dense_z[row, n] = dense_in[:, free]
                free += 1

    looked_up = [2 * k + i for k in LOOKED_UP for i in range(2)]
    rows = [inputs[f"tbl_{f}"].shape[0] // TP for f in looked_up]
    minus_first_row = -np.arange(TP, dtype=np.float32)[:, None] * np.array(rows, np.float32)

    arrays = {
        "dense_z": dense_z,
        "ids": np.ascontiguousarray(inputs["ids"]),
        "ids_up": np.ascontiguousarray(np.asarray(inputs["ids"])[:, looked_up].T)[None],
        "minus_first_row": minus_first_row,
        **{f"tbl_{f}": np.ascontiguousarray(inputs[f"tbl_{f}"]) for f in range(FIELDS)},
        "k_tiles": k_tiles.reshape(NQ, P, CC),
        "w1": w1,
        "w2": np.ascontiguousarray(np.asarray(inputs["W_top2"]).reshape(M1, P, HID2).transpose(1, 0, 2)),
        "w3": np.ascontiguousarray(np.asarray(inputs["W_top3"]).reshape(M2, P).T),
        "b1": np.ascontiguousarray(np.asarray(inputs["b_top1"]).reshape(M1, P).T),
        "b2": np.ascontiguousarray(np.asarray(inputs["b_top2"]).reshape(M2, P).T),
    }
    nc = bacc.Bacc("TRN2", target_bir_lowering=False, num_devices=1)
    ap = {n: nc.dram_tensor(n, a.shape, mybir.dt.from_np(a.dtype), kind="ExternalInput").ap()
          for n, a in arrays.items()}
    y = nc.dram_tensor("y", (BATCH, 1), F32, kind="ExternalOutput").ap()
    dlrm_tower(nc, ap["dense_z"], ap["ids"], ap["ids_up"], ap["minus_first_row"], [ap[f"tbl_{f}"] for f in range(FIELDS)], ap["k_tiles"],
               ap["w1"], ap["w2"], ap["w3"], ap["b1"], ap["b2"], y)
    return run_bass_kernel_spmd(nc, [arrays], core_ids=[0]).results[0]["y"]
```
